# Optimizing a Trainium2 kernel written in Bass

```python
import numpy as np
import jax
import jax.numpy as jnp

def _softmax(x, axis=-1):
    return jax.nn.softmax(x, axis=axis)

def _gelu(x):
    return jax.nn.gelu(x, approximate=True)

def _silu(x):
    return jax.nn.silu(x)

def _sigmoid(x):
    return jax.nn.sigmoid(x)

def _layernorm(x, axis=-1, eps=1e-05):
    m = jnp.mean(x, axis=axis, keepdims=True)
    v = jnp.var(x, axis=axis, keepdims=True)
    return (x - m) / jnp.sqrt(v + eps)

def _scatter_add(tgt, idx, src, axis=0):
    return tgt.at[idx].add(src)

def _segment_sum(src, seg, n):
    return jax.ops.segment_sum(src, seg, n)
kernel_name = 'mk_macaron_d2_jaxref_r4_6942e6'

def setup_inputs(seed: int=0):
    np.random.seed(seed)
    _w = jnp.asarray

    def _L0_attn_setup():
        import jax, jax.numpy as jnp
        import numpy as np
        N_HEAD = 16
        N_LANDMARKS = 64
        N_ITER = 6

        def _landmarks(t, nL):
            B, nh, T, hs = t.shape
            return t.reshape(B, nh, nL, T // nL, hs).mean(axis=3)

        def _iterative_inv(K, n_iter=N_ITER):
            I = jnp.eye(K.shape[-1], dtype=K.dtype)
            denom = jnp.max(jnp.sum(K, axis=-2), axis=-1)[..., None, None]
            V = K.swapaxes(-1, -2) / denom
            for _ in range(n_iter):
                KV = K @ V
                V = 0.25 * V @ (13.0 * I - KV @ (15.0 * I - KV @ (7.0 * I - KV)))
            return V
        key = jax.random.key(seed)
        k1, k2, k3 = jax.random.split(key, 3)
        B, T, C = (4, 1024, 256)
        x = jax.random.normal(k1, (B, T, C), dtype=jnp.float32)
        W_attn = jax.random.normal(k2, (C, 3 * C), dtype=jnp.float32) * (1.0 / np.sqrt(C))
        W_proj = jax.random.normal(k3, (C, C), dtype=jnp.float32) * (1.0 / np.sqrt(C))
        return {'x': x, 'W_attn': W_attn, 'W_proj': W_proj}
    _L0_attn_in = _L0_attn_setup()

    def _L0_ffn_setup():
        import jax, jax.numpy as jnp
        import numpy as np
        import math
        D_MODEL = 256
        D_FF = 1024
        NUM_EXPERTS = 8
        NUM_SHARED = 1
        E_ROUTED = NUM_EXPERTS - NUM_SHARED
        TOP_K = 2
        CAP_FACTOR = 1.25
        B, S = (4, 512)
        T = B * S
        CAPACITY = math.ceil(CAP_FACTOR * T * TOP_K / E_ROUTED)
        SHARED_SCALE = 1.0

        def _layernorm(x, g, b, eps=1e-05):
            mu = jnp.mean(x, axis=-1, keepdims=True)
            var = jnp.mean((x - mu) ** 2, axis=-1, keepdims=True)
            return (x - mu) * jax.lax.rsqrt(var + eps) * g + b
        key = jax.random.key(seed)
        ks = jax.random.split(key, 10)
        s = 0.02
        return {'x': jax.random.normal(ks[0], (B, S, D_MODEL), dtype=jnp.float32), 'ln_g': jnp.ones((D_MODEL,), jnp.float32), 'ln_b': jnp.zeros((D_MODEL,), jnp.float32), 'Wr': jax.random.normal(ks[1], (D_MODEL, E_ROUTED), jnp.float32) * s, 'W1': jax.random.normal(ks[2], (E_ROUTED, D_MODEL, D_FF), jnp.float32) * s, 'W3': jax.random.normal(ks[3], (E_ROUTED, D_MODEL, D_FF), jnp.float32) * s, 'W2': jax.random.normal(ks[4], (E_ROUTED, D_FF, D_MODEL), jnp.float32) * s, 'W1s': jax.random.normal(ks[5], (D_MODEL, D_FF), jnp.float32) * s, 'W3s': jax.random.normal(ks[6], (D_MODEL, D_FF), jnp.float32) * s, 'W2s': jax.random.normal(ks[7], (D_FF, D_MODEL), jnp.float32) * s}
    _L0_ffn_in = _L0_ffn_setup()

    def _L1_attn_setup():
        import jax, jax.numpy as jnp
        import numpy as np
        EMBED_DIM = 256
        NUM_HEADS = 16

        def quat_norm(q, eps=1e-06):
            r, i, j, k = jnp.split(q, 4, axis=-1)
            n = jnp.sqrt(r * r + i * i + j * j + k * k + eps)
            return jnp.concatenate([r / n, i / n, j / n, k / n], axis=-1)

        def quat_linear(x, W, b):
            B, T, D = x.shape
            D4 = D // 4
            xs = x.reshape(B, T, 4, D4)
            A = jnp.einsum('btcd,wdo->btcwo', xs, W) + b
            r = A[:, :, 0, 0] - A[:, :, 1, 1] - A[:, :, 2, 2] - A[:, :, 3, 3]
            i = A[:, :, 1, 0] + A[:, :, 0, 1] + A[:, :, 3, 2] - A[:, :, 2, 3]
            j = A[:, :, 2, 0] - A[:, :, 3, 1] + A[:, :, 0, 2] + A[:, :, 1, 3]
            k = A[:, :, 3, 0] + A[:, :, 2, 1] - A[:, :, 1, 2] + A[:, :, 0, 3]
            return jnp.concatenate([r, i, j, k], axis=-1)
        key = jax.random.key(seed)
        ks = jax.random.split(key, 10)
        B, T, D = (2, 512, EMBED_DIM)
        D4 = D // 4
        s = 0.02
        x = jax.random.normal(ks[0], (B, T, D), dtype=jnp.float32)

        def proj(kw, kb):
            W = jax.random.normal(kw, (4, D4, D4), dtype=jnp.float32) * s
            b = jax.random.normal(kb, (4, D4), dtype=jnp.float32) * s
            return (W, b)
        qW, qb = proj(ks[1], ks[2])
        kW, kb = proj(ks[3], ks[4])
        vW, vb = proj(ks[5], ks[6])
        oW, ob = proj(ks[7], ks[8])
        J = jax.random.normal(ks[9], (D,), dtype=jnp.float32) * 0.01
        return {'x': x, 'qW': qW, 'qb': qb, 'kW': kW, 'kb': kb, 'vW': vW, 'vb': vb, 'oW': oW, 'ob': ob, 'J': J}
    _L1_attn_in = _L1_attn_setup()

    def _L1_ffn_setup():
        import jax, jax.numpy as jnp
        import numpy as np
        B, N, D, E, DFF = (4, 512, 256, 16, 1024)
        CAPACITY_FACTOR = 2.0
        CAP = int(N * CAPACITY_FACTOR / E)
        SINKHORN_ITERS = 6

        def _sinkhorn(logits, n_iters=SINKHORN_ITERS, tau=1.0):
            t = logits / tau
            for _ in range(n_iters):
                t = t - jax.scipy.special.logsumexp(t, axis=-2, keepdims=True)
                t = t - jax.scipy.special.logsumexp(t, axis=-1, keepdims=True)
            return jnp.exp(t)
        key = jax.random.key(seed)
        ks = jax.random.split(key, 6)
        scaled = lambda k, sh, fan: (jax.random.normal(k, sh, jnp.float32) / np.sqrt(fan)).astype(jnp.float32)
        return {'x': jax.random.normal(ks[0], (B, N, D), jnp.float32), 'gate_query': scaled(ks[1], (E, D), D), 'log_temp': jnp.asarray(np.log(0.5), jnp.float32), 'w1': scaled(ks[2], (E, D, DFF), D), 'b1': jnp.zeros((E, DFF), jnp.float32), 'w2': scaled(ks[3], (E, DFF, D), DFF), 'b2': jnp.zeros((E, D), jnp.float32)}
    _L1_ffn_in = _L1_ffn_setup()
    _d = {'L0_attn_x': _L0_attn_in['x'], 'L0_attn_W_attn': _L0_attn_in['W_attn'], 'L0_attn_W_proj': _L0_attn_in['W_proj'], 'L0_ffn_ln_g': _L0_ffn_in['ln_g'], 'L0_ffn_ln_b': _L0_ffn_in['ln_b'], 'L0_ffn_Wr': _L0_ffn_in['Wr'], 'L0_ffn_W1': _L0_ffn_in['W1'], 'L0_ffn_W3': _L0_ffn_in['W3'], 'L0_ffn_W2': _L0_ffn_in['W2'], 'L0_ffn_W1s': _L0_ffn_in['W1s'], 'L0_ffn_W3s': _L0_ffn_in['W3s'], 'L0_ffn_W2s': _L0_ffn_in['W2s'], 'L1_attn_qW': _L1_attn_in['qW'], 'L1_attn_qb': _L1_attn_in['qb'], 'L1_attn_kW': _L1_attn_in['kW'], 'L1_attn_kb': _L1_attn_in['kb'], 'L1_attn_vW': _L1_attn_in['vW'], 'L1_attn_vb': _L1_attn_in['vb'], 'L1_attn_oW': _L1_attn_in['oW'], 'L1_attn_ob': _L1_attn_in['ob'], 'L1_attn_J': _L1_attn_in['J'], 'L1_ffn_gate_query': _L1_ffn_in['gate_query'], 'L1_ffn_log_temp': _L1_ffn_in['log_temp'], 'L1_ffn_w1': _L1_ffn_in['w1'], 'L1_ffn_b1': _L1_ffn_in['b1'], 'L1_ffn_w2': _L1_ffn_in['w2'], 'L1_ffn_b2': _L1_ffn_in['b2']}
    _x0 = _d['L0_attn_x']
    _d['L0_attn_x'] = jax.random.normal(jax.random.fold_in(jax.random.key(seed), 1), (4, 1024, 256), dtype=_x0.dtype)
    del _x0
    return _d

def reference(L0_attn_x, L0_attn_W_attn, L0_attn_W_proj, L0_ffn_ln_g, L0_ffn_ln_b, L0_ffn_Wr, L0_ffn_W1, L0_ffn_W3, L0_ffn_W2, L0_ffn_W1s, L0_ffn_W3s, L0_ffn_W2s, L1_attn_qW, L1_attn_qb, L1_attn_kW, L1_attn_kb, L1_attn_vW, L1_attn_vb, L1_attn_oW, L1_attn_ob, L1_attn_J, L1_ffn_gate_query, L1_ffn_log_temp, L1_ffn_w1, L1_ffn_b1, L1_ffn_w2, L1_ffn_b2):

    def _L0_attn_ref(x, W_attn, W_proj):
        import jax, jax.numpy as jnp
        import numpy as np
        N_HEAD = 16
        N_LANDMARKS = 64
        N_ITER = 6

        def _landmarks(t, nL):
            B, nh, T, hs = t.shape
            return t.reshape(B, nh, nL, T // nL, hs).mean(axis=3)

        def _iterative_inv(K, n_iter=N_ITER):
            I = jnp.eye(K.shape[-1], dtype=K.dtype)
            denom = jnp.max(jnp.sum(K, axis=-2), axis=-1)[..., None, None]
            V = K.swapaxes(-1, -2) / denom
            for _ in range(n_iter):
                KV = K @ V
                V = 0.25 * V @ (13.0 * I - KV @ (15.0 * I - KV @ (7.0 * I - KV)))
            return V
        B, T, C = x.shape
        nh, nL = (N_HEAD, N_LANDMARKS)
        hs = C // nh
        qkv = x @ W_attn
        q, k, v = jnp.split(qkv, 3, axis=-1)

        def heads(t):
            return t.reshape(B, T, nh, hs).transpose(0, 2, 1, 3)
        q, k, v = (heads(q), heads(k), heads(v))
        q_l = _landmarks(q, nL)
        k_l = _landmarks(k, nL)
        L = jax.nn.softmax(jnp.einsum('bhtd,bhld->bhtl', q, k_l), axis=-1)
        P = _iterative_inv(jax.nn.softmax(jnp.einsum('bhld,bhmd->bhlm', q_l, k_l), axis=-1))
        N = jax.nn.softmax(jnp.einsum('bhld,bhtd->bhlt', q_l, k), axis=-1)
        y = L @ (P @ (N @ v))
        y = y.transpose(0, 2, 1, 3).reshape(B, T, C)
        return y @ W_proj

    def _L0_ffn_ref(x, ln_g, ln_b, Wr, W1, W3, W2, W1s, W3s, W2s):
        import jax, jax.numpy as jnp
        import numpy as np
        import math
        D_MODEL = 256
        D_FF = 1024
        NUM_EXPERTS = 8
        NUM_SHARED = 1
        E_ROUTED = NUM_EXPERTS - NUM_SHARED
        TOP_K = 2
        CAP_FACTOR = 1.25
        B, S = (4, 512)
        T = B * S
        CAPACITY = math.ceil(CAP_FACTOR * T * TOP_K / E_ROUTED)
        SHARED_SCALE = 1.0

        def _layernorm(x, g, b, eps=1e-05):
            mu = jnp.mean(x, axis=-1, keepdims=True)
            var = jnp.mean((x - mu) ** 2, axis=-1, keepdims=True)
            return (x - mu) * jax.lax.rsqrt(var + eps) * g + b
        Bx, Sx, D = x.shape
        Tn = Bx * Sx
        h = _layernorm(x, ln_g, ln_b).reshape(Tn, D)
        logits = h @ Wr
        top_vals, top_idx = jax.lax.top_k(logits, TOP_K)
        gates = jax.nn.softmax(top_vals, axis=-1)
        idx = top_idx.T.reshape(-1)
        gat = gates.T.reshape(-1)
        tok = jnp.tile(jnp.arange(Tn), TOP_K)
        onehot = jax.nn.one_hot(idx, E_ROUTED, dtype=jnp.int32)
        pos = jnp.sum(jnp.cumsum(onehot, axis=0) * onehot, axis=-1) - 1
        keep = pos < CAPACITY
        pos_c = jnp.where(keep, pos, CAPACITY)
        xe = jnp.zeros((E_ROUTED, CAPACITY, D), h.dtype).at[idx, pos_c].set(h[tok], mode='drop')
        a = jnp.einsum('ecd,edf->ecf', xe, W1)
        b = jnp.einsum('ecd,edf->ecf', xe, W3)
        ye = jnp.einsum('ecf,efd->ecd', jax.nn.silu(a) * b, W2)
        out_slots = ye[jnp.clip(idx, 0, E_ROUTED - 1), jnp.clip(pos_c, 0, CAPACITY - 1)]
        out_slots = out_slots * (gat * keep.astype(gat.dtype))[:, None]
        routed = jnp.zeros((Tn, D), h.dtype).at[tok].add(out_slots)
        shared = jax.nn.silu(h @ W1s) * (h @ W3s) @ W2s
        out = routed + SHARED_SCALE * shared
        return out.reshape(Bx, Sx, D)

    def _L1_attn_ref(x, qW, qb, kW, kb, vW, vb, oW, ob, J):
        import jax, jax.numpy as jnp
        import numpy as np
        EMBED_DIM = 256
        NUM_HEADS = 16

        def quat_norm(q, eps=1e-06):
            r, i, j, k = jnp.split(q, 4, axis=-1)
            n = jnp.sqrt(r * r + i * i + j * j + k * k + eps)
            return jnp.concatenate([r / n, i / n, j / n, k / n], axis=-1)

        def quat_linear(x, W, b):
            B, T, D = x.shape
            D4 = D // 4
            xs = x.reshape(B, T, 4, D4)
            A = jnp.einsum('btcd,wdo->btcwo', xs, W) + b
            r = A[:, :, 0, 0] - A[:, :, 1, 1] - A[:, :, 2, 2] - A[:, :, 3, 3]
            i = A[:, :, 1, 0] + A[:, :, 0, 1] + A[:, :, 3, 2] - A[:, :, 2, 3]
            j = A[:, :, 2, 0] - A[:, :, 3, 1] + A[:, :, 0, 2] + A[:, :, 1, 3]
            k = A[:, :, 3, 0] + A[:, :, 2, 1] - A[:, :, 1, 2] + A[:, :, 0, 3]
            return jnp.concatenate([r, i, j, k], axis=-1)
        B, T, D = x.shape
        H = NUM_HEADS
        Dh = D // H
        scale = Dh ** (-0.5)
        q = quat_norm(quat_linear(x, qW, qb))
        k = quat_norm(quat_linear(x, kW, kb))
        v = quat_linear(x, vW, vb)
        q_ = q.reshape(B, T, H, Dh)
        k_ = k.reshape(B, T, H, Dh)
        v_ = v.reshape(B, T, H, Dh)
        scores = jnp.einsum('bthd,bshd->bhts', q_, k_) * scale
        scores = scores + jnp.mean(jnp.sin(J[:T])) * 0.1
        attn = jax.nn.softmax(scores, axis=-1)
        out = jnp.einsum('bhts,bshd->bthd', attn, v_).reshape(B, T, D)
        return quat_linear(out, oW, ob)

    def _L1_ffn_ref(x, gate_query, log_temp, w1, b1, w2, b2):
        import jax, jax.numpy as jnp
        import numpy as np
        B, N, D, E, DFF = (4, 512, 256, 16, 1024)
        CAPACITY_FACTOR = 2.0
        CAP = int(N * CAPACITY_FACTOR / E)
        SINKHORN_ITERS = 6

        def _sinkhorn(logits, n_iters=SINKHORN_ITERS, tau=1.0):
            t = logits / tau
            for _ in range(n_iters):
                t = t - jax.scipy.special.logsumexp(t, axis=-2, keepdims=True)
                t = t - jax.scipy.special.logsumexp(t, axis=-1, keepdims=True)
            return jnp.exp(t)
        b, n, d = x.shape
        gate_logits = jnp.einsum('bnd,ed->ben', x, gate_query)
        affinity_logits = gate_logits / jnp.exp(log_temp)
        affinity = _sinkhorn(affinity_logits)
        gates, idx = jax.lax.top_k(affinity, CAP)
        expert_in = jnp.take_along_axis(x[:, None, :, :], idx[..., None], axis=2)
        h = jax.nn.gelu(jnp.einsum('becd,edf->becf', expert_in, w1) + b1[None, :, None, :])
        expert_out = jnp.einsum('becf,efd->becd', h, w2) + b2[None, :, None, :]
        out = jnp.zeros_like(x)
        out = out.at[jnp.arange(b)[:, None, None], idx].add(gates[..., None] * expert_out)
        return out
    x = L0_attn_x
    x = x + 0.5 * _L0_ffn_ref(_layernorm(x, axis=-1), L0_ffn_ln_g, L0_ffn_ln_b, L0_ffn_Wr, L0_ffn_W1, L0_ffn_W3, L0_ffn_W2, L0_ffn_W1s, L0_ffn_W3s, L0_ffn_W2s)
    x = x + _L0_attn_ref(_layernorm(x, axis=-1), L0_attn_W_attn, L0_attn_W_proj)
    x = x + 0.5 * _L0_ffn_ref(_layernorm(x, axis=-1), L0_ffn_ln_g, L0_ffn_ln_b, L0_ffn_Wr, L0_ffn_W1, L0_ffn_W3, L0_ffn_W2, L0_ffn_W1s, L0_ffn_W3s, L0_ffn_W2s)
    x = x + 0.5 * _L1_ffn_ref(_layernorm(x, axis=-1), L1_ffn_gate_query, L1_ffn_log_temp, L1_ffn_w1, L1_ffn_b1, L1_ffn_w2, L1_ffn_b2)
    x = x + _L1_attn_ref(_layernorm(x, axis=-1), L1_attn_qW, L1_attn_qb, L1_attn_kW, L1_attn_kb, L1_attn_vW, L1_attn_vb, L1_attn_oW, L1_attn_ob, L1_attn_J)
    x = x + 0.5 * _L1_ffn_ref(_layernorm(x, axis=-1), L1_ffn_gate_query, L1_ffn_log_temp, L1_ffn_w1, L1_ffn_b1, L1_ffn_w2, L1_ffn_b2)
    return x

_drawn_inputs = setup_inputs


def setup_inputs(seed=0):
    import zlib

    import numpy as np

    out = dict(_drawn_inputs(seed))
    spreads = {'L0_ffn_ln_g': (1.0, 0.6),
     'L0_ffn_ln_b': (0.0, 0.8),
     'L1_ffn_b1': (0.0, 0.8),
     'L1_ffn_b2': (0.0, 0.8)}
    factors = {'L0_ffn_Wr': 2.987,
     'L0_ffn_W1': 2.712,
     'L0_ffn_W3': 2.676,
     'L0_ffn_W2': 2.679,
     'L1_attn_qW': 8.0,
     'L1_attn_qb': 8.0,
     'L1_attn_kW': 8.0,
     'L1_attn_kb': 8.0,
     'L1_attn_vW': 8.0,
     'L1_attn_vb': 4.331,
     'L1_attn_oW': 3.954,
     'L1_ffn_gate_query': 8.0,
     'L1_ffn_w1': 8.0,
     'L1_ffn_w2': 8.0}
    for name, (base, spread) in spreads.items():
        noise = np.random.default_rng([zlib.crc32(name.encode()), seed]).standard_normal(out[name].shape)
        drawn = base * np.exp(spread * noise) if base else spread * noise
        out[name] = jnp.asarray(drawn.astype(out[name].dtype))
    for name, factor in factors.items():
        out[name] = (out[name] * factor).astype(out[name].dtype)
    return out
```

```python
import numpy as np
import concourse.bass as bass
from concourse import mybir
from contextlib import ExitStack

F32 = mybir.dt.float32
BF16 = mybir.dt.bfloat16
U32 = mybir.dt.uint32
ALU = mybir.AluOpType
ACT = mybir.ActivationFunctionType
AX = mybir.AxisListType.X


class Tok:

    def __init__(self, lane, sem=None, val=0):
        self.lane, self.sem, self.val, self.used = lane, sem, val, False


def flat(waits):
    for w in waits:
        if w is None:
            continue
        if isinstance(w, Tok):
            yield w
        else:
            yield from flat(w)


class Lane:

    def __init__(self, nc, name, ctx, ndma=0):
        self.nc, self.name, self.q = nc, name, []
        self.sem = ctx.enter_context(nc.semaphore("s_" + name))
        self.last = None
        self.pending = []
        self.dsems = [ctx.enter_context(nc.semaphore(f"d_{name}{i}")) for i in range(ndma)]
        self.dlast = [None] * ndma
        self.dn = 0

    def __call__(self, fn, *waits):
        t = Tok(self)
        ws = list(flat(waits)) + self.pending
        if self.name == "pool" and self.last:
            ws.append(self.last)
        self.pending = []
        for w in ws:
            w.used = True
        self.q.append((fn, ws, t, 1))
        self.last = t
        return t

    def dma(self, fn, *waits):
        i = self.dn % len(self.dsems)
        self.dn += 1
        old = self.dlast[i]
        t = Tok(None, self.dsems[i], (old.val if old else 0) + 16)
        ws = list(flat(waits)) + self.pending + ([old] if old else [])
        self.pending = []
        for w in ws:
            w.used = True
        self.dlast[i] = t
        self.q.append((fn, ws, t, 16))
        return t

    def count(self):
        n = 0
        for _, _, t, by in self.q:
            if by == 1 and t.used:
                n += 1
                t.sem, t.val = self.sem, n

    def replay(self, e):
        known = {}
        for fn, ws, t, by in self.q:
            need = {}
            for w in ws:
                if w.lane is self and self.name == "pe":
                    continue
                k = id(w.sem)
                if known.get(k, 0) < w.val and need.get(k, (None, 0))[1] < w.val:
                    need[k] = (w.sem, w.val)
            for k, (s, v) in need.items():
                e.wait_ge(s, v)
                known[k] = v
            ins = fn(e)
            if by == 16:
                ins.then_inc(t.sem, 16)
            elif t.used:
                ins.then_inc(t.sem, 1)


class Ring:

    def __init__(self, views):
        self.views, self.free, self.n = views, [[] for _ in views], 0

    def take(self):
        i = self.n % len(self.views)
        self.n += 1
        w = self.free[i]
        assert w is not None, "taken before it was given back"
        self.free[i] = None
        return i, self.views[i], w

    def give(self, i, *toks):
        self.free[i] = list(flat(toks))


def macaron_kernel(nc, A, out, span=(0, 6)):
    ctx = ExitStack()
    with ctx:
        T, NT, D, FF = 4096, 32, 256, 1024
        E0, CAP0 = 7, 732
        X = ctx.enter_context(nc.sbuf_tensor("X", [128, NT, D], F32))
        Z = ctx.enter_context(nc.sbuf_tensor("Z", [128, NT, D], F32))
        HT = ctx.enter_context(nc.sbuf_tensor("HT", [128, 2, T], F32))
        WK = ctx.enter_context(nc.sbuf_tensor("WK", [128, 27300], F32))
        IDENT = ctx.enter_context(nc.sbuf_tensor("IDENT", [128, 128], F32))
        ONES = ctx.enter_context(nc.sbuf_tensor("ONES", [128, 128], F32))
        SM = ctx.enter_context(nc.sbuf_tensor("SM", [128, 960], F32))
        PS = ctx.enter_context(nc.psum_tensor("PS", [128, 8, 512], F32))
        XE = nc.dram_tensor("xe_scratch", (E0 * CAP0, D), F32, kind="Internal").ap()
        YE = nc.dram_tensor("ye_scratch", (E0 * CAP0, D), F32, kind="Internal").ap()
        XN = nc.dram_tensor("xn_scratch", (T, D), F32, kind="Internal").ap()

        pe = Lane(nc, "pe", ctx)
        act = Lane(nc, "act", ctx)
        dve = Lane(nc, "dve", ctx)
        pool = Lane(nc, "pool", ctx, 16)
        sp = Lane(nc, "sp", ctx, 24)
        lanes = [pe, act, dve, pool, sp]

        def barrier():
            toks = [ln.last for ln in lanes if ln.last] + [t for ln in lanes for t in ln.dlast if t]
            for t in toks:
                t.used = True
            for ln in lanes:
                ln.pending = list(toks)
            return toks

        def w(off, *shape):
            n = int(np.prod(shape))
            v = WK[:, off:off + n]
            if len(shape) == 1:
                return v
            names = "abcd"[:len(shape)]
            return v.rearrange(f"p ({' '.join(names)}) -> p {' '.join(names)}",
                               **{c: s for c, s in zip(names[1:], shape[1:])})

        sm_at = [0]

        def sm(*shape):
            n = int(np.prod(shape))
            off = sm_at[0]
            sm_at[0] += n
            assert sm_at[0] <= 960
            v = SM[:, off:off + n]
            if len(shape) == 1:
                return v
            names = "abcd"[:len(shape)]
            return v.rearrange(f"p ({' '.join(names)}) -> p {' '.join(names)}",
                               **{c: s for c, s in zip(names[1:], shape[1:])})

        def bank(i, n=512):
            return PS[:, i, 0:n]

        def pair(i):
            return PS[:, i:i + 2, :].rearrange("p a b -> p (a b)")

        def mm(o, l, r, start, stop, *waits):
            return pe(lambda e: e.matmul(o, l, r, start=start, stop=stop, skip_group_check=True), *waits)

        def tr(o, i, *waits):
            k = i.shape[0]
            return pe(lambda e: e.transpose(o, i, IDENT[0:k, 0:k]), *waits)

        def act_f(o, i, f, *waits, bias=0.0, scale=1.0, acc=None):
            return act(lambda e: e.activation(o, i, f, bias=bias, scale=scale, accum_out=acc), *waits)

        def cp(ln, o, i, *waits):
            if ln is act:
                return act(lambda e: e.activation(o, i, ACT.Copy), *waits)
            return ln(lambda e: e.tensor_copy(o, i), *waits)

        def tt(ln, o, a, b, op, *waits):
            return ln(lambda e: e.tensor_tensor(o, a, b, op), *waits)

        def ts(ln, o, a, s1, s2, op0, op1, *waits):
            if s2 is None:
                return ln(lambda e: e.tensor_scalar(o, a, s1, None, op0), *waits)
            return ln(lambda e: e.tensor_scalar(o, a, s1, s2, op0, op1), *waits)

        def stt(o, a, s, b, op0, op1, *waits):
            return dve(lambda e: e.scalar_tensor_tensor(o, a, s, b, op0, op1), *waits)

        def red(o, i, op, *waits):
            return dve(lambda e: e.tensor_reduce(o, i, AX, op), *waits)

        def rcp(o, i, *waits):
            return dve(lambda e: e.reciprocal(o, i), *waits)

        def mset(ln, o, v, *waits):
            return ln(lambda e: e.memset(o, v), *waits)

        def asel(o, pattern, op, fill, base, cm, *waits):
            return pool(lambda e: e.affine_select(out=o, in_=o, pattern=pattern, compare_op=op, fill=fill,
                                                  base=base, channel_multiplier=cm), *waits)

        def iota(o, pattern, base, cm, *waits):
            return pool(lambda e: e.iota(o, pattern, base=base, channel_multiplier=cm,
                                         allow_small_or_imprecise_dtypes=True), *waits)

        t = mset(pool, IDENT[:, :], 0.0)
        t_id = asel(IDENT[:, :], [[-1, 128]], ALU.not_equal, 1.0, 0, 1, t)
        t_ones = mset(pool, ONES[:, :], 1.0)
        xv = A["L0_attn_x"].rearrange("b (i p) d -> p (b i) d", p=128)
        tX = []
        for g in range(4):
            t = sp.dma(lambda e, g=g: e.dma_start(X[:, 8 * g:8 * g + 8, :], xv[:, 8 * g:8 * g + 8, :]))
            tX += [[t]] * 8

        ST = sm(8, 6)
        MV = sm(NT, 2)
        R = sm(NT)
        S1, S2, S3, S4 = sm(8), sm(8), sm(8), sm(8)
        GB = sm(2, 2)
        sm_keep = sm_at[0]

        def rsqrt(o, v, *waits):
            t = act_f(S2, v, ACT.Sqrt, *waits)
            t = rcp(o, S2, t)
            t = tt(dve, S3, o, o, ALU.mult, t)
            t = tt(dve, S3, S3, v, ALU.mult, t)
            t = ts(dve, S3, S3, -0.5, 1.5, ALU.mult, ALU.add, t)
            return tt(dve, o, o, S3, ALU.mult, t)

        def layernorm(twice, gb, psum, bar):
            tz, th = [], []
            prev = []
            for g in range(4):
                r8 = R[:, 8 * g:8 * g + 8]
                v8 = MV[:, 8 * g:8 * g + 8, 1]
                ta = []
                for i in range(8 * g, 8 * g + 8):
                    t = dve(lambda e, i=i: e.bn_stats(ST[:, i % 8, :], X[:, i, :]), tX[i], prev)
                    ta.append(dve(lambda e, i=i: e.bn_aggr(MV[:, i, :], ST[:, i % 8, :]), t))
                t = ts(dve, S1, v8, 1e-5, None, ALU.add, None, ta, prev)
                t = rsqrt(r8, S1, t)
                if twice:
                    t = tt(dve, S4, v8, r8, ALU.mult, t)
                    t = tt(dve, S4, S4, r8, ALU.mult, t)
                    t = ts(dve, S1, S4, 1e-5, None, ALU.add, None, t)
                    t = rsqrt(S4, S1, t)
                    t = tt(dve, r8, r8, S4, ALU.mult, t)
                prev = [t]
                for i in range(8 * g, 8 * g + 8):
                    tz.append(ts(dve, Z[:, i, :], X[:, i, :], MV[:, i, 0:1], R[:, i:i + 1],
                                 ALU.subtract, ALU.mult, t))
                for h in range(2 * g, 2 * g + 2):
                    te = []
                    for c in range(2):
                        n, b, wt = psum.take()
                        for k in range(4):
                            i = 4 * h + k
                            t = tr(b[:, 128 * k:128 * k + 128], Z[:, i, 128 * c:128 * c + 128], tz[i], wt, t_id)
                        dst = HT[:, c, 512 * h:512 * h + 512]
                        if gb is not None:
                            t = act_f(dst, b, ACT.Identity, t, gb, bias=GB[:, 1, c:c + 1], scale=GB[:, 0, c:c + 1])
                        else:
                            t = cp(act, dst, b, t)
                        psum.give(n, t)
                        te.append(t)
                    th.append(te)
            return tz, th

        def load(dst, src, *waits):
            return sp.dma(lambda e: e.dma_start(dst, src, allow_slow_non_contiguous=True), *waits)

        def cpf(src):
            return src.rearrange("(c p) f -> p c f", p=128)

        def ffn0(first):
            bar = barrier()
            sm_at[0] = sm_keep
            ROWG, ROWS = sm(64), sm(64)
            GT = sm(2, NT)
            psum = Ring([bank(i) for i in range(8)])
            tgb = [load(GB[:, 0, :], A["L0_ffn_ln_g"].rearrange("(c p) -> p c", p=128)),
                   load(GB[:, 1, :], A["L0_ffn_ln_b"].rearrange("(c p) -> p c", p=128))]

            def wslot(s):
                o = 6144 * s
                return w(o, 2, FF), w(o + 2048, 2, FF), w(o + 4096, 8, D)

            wfree = [[], []]

            def wload(s, w1, w3, w2):
                a, b, c = wslot(s)
                return [load(a, cpf(w1), wfree[s]), load(b, cpf(w3), wfree[s]), load(c, cpf(w2), wfree[s])]

            WR = w(27216, 2, 7)
            twr = load(WR, cpf(A["L0_ffn_Wr"]))
            tws = wload(0, A["L0_ffn_W1s"], A["L0_ffn_W3s"], A["L0_ffn_W2s"])
            twe = [wload(1, A["L0_ffn_W1"][0], A["L0_ffn_W3"][0], A["L0_ffn_W2"][0])]
            tzero = []
            if first:
                ZR = w(25680, 1536)
                t = mset(pool, ZR, 0.0)
                for e_ in range(E0):
                    tzero.append(load(XE[e_ * CAP0:(e_ + 1) * CAP0, :].rearrange("(p t) d -> p (t d)", t=6),
                                      ZR[0:122, :], t))
            tz, th = layernorm(True, tgb, psum, bar)
            n, LB, wt = psum.take()
            for i in range(NT):
                for c in range(2):
                    tl = mm(LB[:, 8 * i:8 * i + 7], HT[:, c, 128 * i:128 * i + 128], WR[:, c, :],
                            c == 0, c == 1, th[i // 4], twr, wt)
            o = 19680
            LG = w(o, NT, 8)
            M8 = w(o + 256, NT, 8)
            I8 = w(o + 512, NT, 8).bitcast(U32)
            IF = w(o + 768, 2, NT)
            IO8 = w(o + 832, 8)
            TRI = w(o + 840, 128)
            OH = w(o + 968, 2, NT, 8)
            TOT = w(o + 1480, 64, 8)
            SC = w(o + 1992, 64, 8)
            POS = w(o + 2504, 64, 8)
            PP = w(o + 3016, 64)
            KP = w(o + 3080, 64)
            EC = w(o + 3144, 64)
            TID = w(o + 3208, 64)
            RF = w(o + 3272, 64)
            O64 = w(o + 3336, 64)
            t_io = iota(IO8, [[1, 8]], 0, 0)
            t_tr = asel(TRI, [[1, 128]], ALU.is_ge, 0.0, 0, -1, mset(pool, TRI, 1.0))
            t_ti = iota(TID, [[128, 64]], 8192, 1)
            t_o6 = mset(pool, O64, 1.0)
            t1 = mset(dve, LG, -3.0e38)
            t = cp(dve, LG[:, :, 0:7], LB[:, 0:256].rearrange("p (i e) -> p i e", e=8)[:, :, 0:7], tl, t1)
            psum.give(n, t)
            tm, ti = [], []
            for i in range(NT):
                a = dve(lambda e, i=i: e.max(M8[:, i, :], LG[:, i, :]), t)
                tm.append(a)
            for i in range(NT):
                ti.append(dve(lambda e, i=i: e.max_index(I8[:, i, :], M8[:, i, :], LG[:, i, :]), tm[i]))
            t = cp(dve, IF, I8[:, :, 0:2].rearrange("p i s -> p s i"), ti)
            toh = []
            for s in range(2):
                toh.append(tt(dve, OH[:, s], IF[:, s, :].unsqueeze(2).broadcast_to([128, NT, 8]),
                              IO8.unsqueeze(1).broadcast_to([128, NT, 8]), ALU.is_equal, t, t_io))
            td = tt(dve, GT[:, 1, :], M8[:, :, 1], M8[:, :, 0], ALU.subtract, tm)
            td = act_f(GT[:, 1, :], GT[:, 1, :], ACT.Exp, td)
            td = ts(dve, GT[:, 0, :], GT[:, 1, :], 1.0, None, ALU.add, None, td)
            td = rcp(GT[:, 0, :], GT[:, 0, :], td)
            tg = tt(dve, GT[:, 1, :], GT[:, 1, :], GT[:, 0, :], ALU.mult, td)
            oh = OH.rearrange("p s i e -> p (s i e)")
            n1, PB, wt1 = psum.take()
            t1 = mm(PB, TRI, oh, True, True, toh, t_tr, wt1)
            n2, TB, wt2 = psum.take()
            t2 = mm(TB, ONES[:, :], oh, True, True, wt2, t_ones)
            t2 = cp(dve, TOT, TB.rearrange("p (a b) -> p a b", b=8), t2)
            psum.give(n2, t2)
            tsc = [dve(lambda e, x=x: e.tensor_tensor_scan(SC[:, :, x], O64, TOT[:, :, x], 0.0, ALU.mult, ALU.add),
                       t2, t_o6) for x in range(8)]
            t = tt(dve, SC, SC, TOT, ALU.subtract, tsc)
            t = tt(dve, SC, SC, PB.rearrange("p (a b) -> p a b", b=8), ALU.add, t, t1)
            psum.give(n1, t)
            oh3 = OH.rearrange("p s i e -> p (s i) e")
            t = tt(dve, POS, SC, oh3, ALU.mult, t)
            t = red(PP, POS, ALU.add, t)
            t = ts(dve, PP, PP, 1.0, None, ALU.subtract, None, t)
            tk = ts(dve, KP, PP, float(CAP0), None, ALU.is_lt, None, t)
            t = ts(dve, EC, IF.rearrange("p s i -> p (s i)"), float(CAP0), None, ALU.mult, None, toh)
            t = tt(dve, PP, PP, EC, ALU.add, t, tk)
            t = tt(dve, PP, PP, KP, ALU.mult, t)
            tr1 = cp(dve, ROWG.bitcast(U32), PP, t)
            t = tt(dve, EC, KP, TID, ALU.mult, t, t_ti)
            t = tt(dve, EC, TID, EC, ALU.subtract, t)
            t = tt(dve, RF, EC, PP, ALU.add, t)
            tr2 = cp(dve, ROWS.bitcast(U32), RF, t)
            gt = GT.rearrange("p s i -> p (s i)")
            t = tt(dve, gt, gt, KP, ALU.mult, tg, tk)
            tgate = ts(dve, gt, gt, 0.5, None, ALU.mult, None, t)
            tsct = []
            for k in range(64):
                i = k % NT
                tsct.append(pool.dma(lambda e, k=k, i=i: e.indirect_dma_start(
                    out=XE, out_offset=bass.IndirectOffsetOnAxis(ap=ROWS.bitcast(U32)[:, k:k + 1], axis=0),
                    in_=Z[:, i, :], in_offset=None, bounds_check=E0 * CAP0 - 1, oob_is_err=False),
                    tr2, tz[i], tzero))
            SIL = Ring([w(18144 + 512 * k, 512) for k in range(3)])
            a, b, c2 = wslot(0)
            HH = w(12288, 8, 512)

            def up(a, b, rhs, N, hdst, tw, tin, hwait):
                n, pa, wt = psum.take()
                n_, pb, wt_ = psum.take()
                for (ww, pp, wx) in ((a, pa, wt), (b, pb, wt_)):
                    for c in range(2):
                        t = mm(pp[:, 0:N], ww[c], rhs[c], c == 0, c == 1, wx, tw, tin)
                    if ww is a:
                        ta = t
                m, sl, ws = SIL.take()
                t1 = act_f(sl[:, 0:N], pa[:, 0:N], ACT.Silu, ta, ws)
                psum.give(n, t1)
                t2 = tt(dve, hdst, sl[:, 0:N], pb[:, 0:N], ALU.mult, t1, t, hwait)
                psum.give(n_, t2)
                SIL.give(m, t2)
                return t2

            hfree = []
            for g in range(8):
                thh = [up([a[:, c, 128 * j:128 * j + 128] for c in range(2)],
                          [b[:, c, 128 * j:128 * j + 128] for c in range(2)],
                          [HT[:, c, 512 * g:512 * g + 512] for c in range(2)], 512, HH[:, j, :], tws, th[g],
                          hfree) for j in range(8)]
                for k in range(4):
                    i = 4 * g + k
                    n, py, wt = psum.take()
                    for j in range(8):
                        t = mm(py[:, 0:D], HH[:, j, 128 * k:128 * k + 128], c2[:, j, :], j == 0, j == 7,
                               thh, wt, tws)
                    t2 = stt(X[:, i, :], py[:, 0:D], 0.5, X[:, i, :], ALU.mult, ALU.add, t, tz[i])
                    psum.give(n, t2)
                    tX[i] = [t2]
                hfree = [t]
            wfree[0] = [t]
            HH = w(12288, 8, CAP0)
            XR = Ring([w(19680 + 1536 * k, 6, D) for k in range(2)])
            XT = Ring([w(22752 + 1464 * k, 2, CAP0) for k in range(2)])
            YO = w(25680, 6, D)
            done_routing = [tgate, tr1, tr2]
            yfree = []
            tye = []
            for e_ in range(E0):
                s = (e_ + 1) % 2
                a, b, c2 = wslot(s)
                if e_ + 1 < E0:
                    twe.append(wload(1 - s, A["L0_ffn_W1"][e_ + 1], A["L0_ffn_W3"][e_ + 1], A["L0_ffn_W2"][e_ + 1]))
                n, xr, wt = XR.take()
                tin = load(xr[0:122], XE[e_ * CAP0:(e_ + 1) * CAP0, :].rearrange("(p t) d -> p t d", t=6),
                           tsct, wt, done_routing)
                m, xt, wx = XT.take()
                txt = []
                for h in range(2):
                    for c in range(2):
                        nb, pb, wb = psum.take()
                        for k in range(3):
                            t = tr(pb[:, 122 * k:122 * k + 122], xr[0:122, 3 * h + k, 128 * c:128 * c + 128],
                                   tin, wb)
                        t2 = act_f(xt[:, c, 366 * h:366 * h + 366], pb[:, 0:366], ACT.Identity, t, wx,
                                   bias=GB[:, 1, c:c + 1], scale=GB[:, 0, c:c + 1])
                        psum.give(nb, t2)
                        txt.append(t2)
                XR.give(n, t)
                thh = []
                for j in range(8):
                    for h in range(2):
                        thh.append(up([a[:, c, 128 * j:128 * j + 128] for c in range(2)],
                                      [b[:, c, 128 * j:128 * j + 128] for c in range(2)],
                                      [xt[:, c, 366 * h:366 * h + 366] for c in range(2)], 366,
                                      HH[:, j, 366 * h:366 * h + 366], twe[e_], txt, hfree))
                XT.give(m, thh)
                ty = []
                for k in range(6):
                    nb, py, wt = psum.take()
                    for j in range(8):
                        t = mm(py[0:122, 0:D], HH[:, j, 122 * k:122 * k + 122], c2[:, j, :], j == 0, j == 7,
                               thh, wt, twe[e_])
                    t2 = cp(act, YO[0:122, k, :], py[0:122, 0:D], t, yfree)
                    psum.give(nb, t2)
                    ty.append(t2)
                hfree = [t]
                wfree[s] = [t]
                t = load(YE[e_ * CAP0:(e_ + 1) * CAP0, :].rearrange("(p t) d -> p t d", t=6), YO[0:122], ty)
                yfree = [t]
                tye.append(t)
            GR = Ring([w(256 * k, 256) for k in range(16)])
            for k in range(64):
                i, s = k // 2, k % 2
                n, gb_, wt = GR.take()
                t = pool.dma(lambda e, i=i, s=s, gb_=gb_: e.indirect_dma_start(
                    out=gb_, out_offset=None, in_=YE,
                    in_offset=bass.IndirectOffsetOnAxis(ap=ROWG.bitcast(U32)[:, NT * s + i:NT * s + i + 1], axis=0)),
                    tye, wt, wfree[0], tr1)
                t2 = stt(X[:, i, :], gb_, GT[:, s, i:i + 1], X[:, i, :], ALU.mult, ALU.add, t, tgate, tX[i])
                GR.give(n, t2)
                tX[i] = [t2]

        def attn0():
            bar = barrier()
            sm_at[0] = sm_keep
            psum = Ring([bank(i) for i in range(8)])
            o = 0
            WA = w(0, 2, 768)
            WP = w(1536, 2, 256)
            BON = w(2048, 128)
            I7, I15, I3 = w(2176, 128), w(2304, 128), w(2432, 128)
            MK = w(2560, 8)
            ZM = w(2568, 32)
            QT = w(2600, 2, 1024)
            KT = w(4648, 2, 1024)
            V = w(6696, 8, 256)
            LM = w(8744, 4, 64)
            BQ = w(9000, 2, 8, 64)
            BK = w(10024, 2, 8, 64)
            KD = w(11048, 8, 128)
            M = w(12072, 8, 128)
            NA = w(13096, 8, 128)
            F = w(14120, 6, 8, 128)
            KN = w(20264, 8, 64)
            KTR = w(20776, 8, 128)
            NE = Ring([w(21800 + 1024 * k, 1024) for k in range(2)])
            ZV = w(23848, 8, 16)
            ZB = w(23976, 8, 32)
            LE = Ring([w(24232 + 512 * k, 8, 64) for k in range(2)])
            LT = Ring([w(25256 + 512 * k, 4, 128) for k in range(2)])
            YN = w(26280, 256)
            YT = w(26536, 256)
            MX, SUMS, DEN = sm(32), sm(32), sm(8)
            NMX, NSUM = sm(8), sm(8)
            LMX, LSM, RIN = sm(2, 8), sm(2, 8), sm(16)
            twa = load(WA, cpf(A["L0_attn_W_attn"]))
            twp = load(WP, cpf(A["L0_attn_W_proj"]))
            t = mset(pool, BON, 0.0)
            t = mset(pool, BON[0:64, 0:64], 1.0, t)
            tc = [mset(pool, BON[64:128, 64:128], 1.0, t)]
            for (v, s) in ((I7, 7.0), (I15, 15.0), (I3, 3.25)):
                tc.append(asel(v, [[-1, 128]], ALU.not_equal, s, 0, 1, mset(pool, v, 0.0)))
            t = mset(pool, MK, 1.0 / 16.0)
            t = asel(MK, [[-16, 8]], ALU.is_ge, 0.0, 0, 1, t)
            tc.append(asel(MK, [[16, 8]], ALU.is_ge, 0.0, 15, -1, t))
            t = mset(pool, ZM, 0.0)
            t = mset(pool, ZM[0:64, 0:16], 1.0, t)
            tc.append(mset(pool, ZM[64:128, 16:32], 1.0, t))
            tc.append(mset(pool, KD, 0.0))
            tz, th = layernorm(False, None, psum, bar)
            NTR = Ring([Z[:, 4 * k:4 * k + 4, :].rearrange("p a b -> p (a b)").rearrange("p (a b) -> p a b", b=128)
                        for k in range(2)])
            tq_free, tv_free = [], []
            prev = []
            for b in range(4):
                H0 = 1024 * b
                tqk = {}
                for which, dst, base in ((0, QT, 0), (1, KT, 256)):
                    for c in range(2):
                        for h in range(2):
                            n, pb, wt = psum.take()
                            for k in range(2):
                                t = mm(pb, WA[:, k, base + 128 * c:base + 128 * c + 128],
                                       HT[:, k, H0 + 512 * h:H0 + 512 * h + 512], k == 0, k == 1,
                                       twa, th[2 * b + h], wt)
                            t = cp(act, dst[:, c, 512 * h:512 * h + 512], pb, t, prev)
                            psum.give(n, t)
                            tqk.setdefault((which, c), []).append(t)
                tv = []
                for i in range(8):
                    n, pb, wt = psum.take()
                    for k in range(2):
                        t = mm(pb[:, 0:256], HT[:, k, H0 + 128 * i:H0 + 128 * i + 128], WA[:, k, 512:768],
                               k == 0, k == 1, twa, th[2 * b + i // 4], wt)
                    t = cp(act, V[:, i, :], pb[:, 0:256], t, prev)
                    psum.give(n, t)
                    tv.append(t)
                tb = {}
                for which, src, B in ((0, QT, BQ), (1, KT, BK)):
                    for c in range(2):
                        lm = LM[:, 2 * which + c, :]
                        t = red(lm, src[:, c, :].rearrange("p (l s) -> p l s", s=16), ALU.add, tqk[which, c], prev)
                        tb[which, c] = tt(dve, B[:, c], lm.unsqueeze(1).broadcast_to([128, 8, 64]),
                                          MK.unsqueeze(2).broadcast_to([128, 8, 64]), ALU.mult, t, tc, prev)
                tkn = []
                for c in range(2):
                    n, pb, wt = psum.take()
                    for k in range(4):
                        q = BQ[:, c, 2 * k:2 * k + 2, :].rearrange("p a b -> p (a b)")
                        kk = BK[:, c, 2 * k:2 * k + 2, :].rearrange("p a b -> p (a b)")
                        t = mm(pb[:, 128 * k:128 * k + 128], q, kk, True, True, tb[0, c], tb[1, c], wt)
                    pv = pb.rearrange("p (k m) -> p k m", m=128)
                    t1 = cp(dve, KN[0:64, 4 * c:4 * c + 4, :], pv[0:64, :, 0:64], t, prev)
                    t2 = cp(dve, KN[64:128, 4 * c:4 * c + 4, :], pv[64:128, :, 64:128], t, prev)
                    psum.give(n, t1, t2)
                    tkn += [t1, t2]
                t = red(MX[:, 0:8], KN, ALU.max, tkn)
                t = tt(dve, KN, KN, MX[:, 0:8].unsqueeze(2).broadcast_to([128, 8, 64]), ALU.subtract, t)
                t = act_f(KN, KN, ACT.Exp, t)
                t = red(SUMS[:, 0:8], KN, ALU.add, t)
                t = rcp(SUMS[:, 0:8], SUMS[:, 0:8], t)
                tkn = tt(dve, KN, KN, SUMS[:, 0:8].unsqueeze(2).broadcast_to([128, 8, 64]), ALU.mult, t)
                n, pb, wt = psum.take()
                t = mm(pb, BON, KN.rearrange("p a b -> p (a b)"), True, True, tkn, tc, wt)
                t = red(DEN, pb.rearrange("p (a b) -> p a b", b=64), ALU.max, t, prev)
                psum.give(n, t)
                tden = rcp(DEN, DEN, t)
                tkd = [cp(dve, KD[0:64, :, 0:64], KN[0:64], tkn, tc, prev),
                       cp(dve, KD[64:128, :, 64:128], KN[64:128], tkn, tc, prev)]
                tkt = []
                for h in range(2):
                    n, pb, wt = psum.take()
                    for k in range(4):
                        t = tr(pb[:, 128 * k:128 * k + 128], KD[:, 4 * h + k, :], tkd, wt)
                    t = cp(act, KTR[:, 4 * h:4 * h + 4, :], pb.rearrange("p (k m) -> p k m", m=128), t, prev)
                    psum.give(n, t)
                    tkt.append(t)
                tM = [None, None]
                for h in range(2):
                    n, pb, wt = psum.take()
                    for k in range(4):
                        kt = KTR[:, 4 * h + k, :]
                        t = mm(pb[:, 128 * k:128 * k + 128], kt, kt, True, True, tkt[h], wt)
                    tM[h] = tt(dve, M[:, 4 * h:4 * h + 4, :], pb.rearrange("p (k m) -> p k m", m=128),
                               DEN[:, 4 * h:4 * h + 4].unsqueeze(2).broadcast_to([128, 4, 128]), ALU.mult,
                               t, tden, prev)
                    psum.give(n, tM[h])
                tF = {}

                def inv_step(it, h, tm):
                    hs = slice(4 * h, 4 * h + 4)
                    bc = lambda I: I.unsqueeze(1).broadcast_to([128, 4, 128])
                    t = stt(NA[:, hs], M[:, hs], -1.0, bc(I7), ALU.mult, ALU.add, tm, tc)
                    for stage in range(2):
                        n, pb, wt = psum.take()
                        for k in range(4):
                            t2 = mm(pb[:, 128 * k:128 * k + 128], M[:, 4 * h + k, :], NA[:, 4 * h + k, :],
                                    True, True, t, tm, wt)
                        pv = pb.rearrange("p (k m) -> p k m", m=128)
                        if stage == 0:
                            t = stt(NA[:, hs], pv, -1.0, bc(I15), ALU.mult, ALU.add, t2)
                        else:
                            t = stt(F[:, it, hs], pv, -0.25, bc(I3), ALU.mult, ALU.add, t2, prev)
                        psum.give(n, t)
                        yield
                    tF[it, h] = t
                    if it == 5:
                        return
                    n, pb, wt = psum.take()
                    for k in range(4):
                        t2 = mm(pb[:, 128 * k:128 * k + 128], M[:, 4 * h + k, :], F[:, it, 4 * h + k, :],
                                True, True, t, tm, wt)
                    tm[:] = [cp(act, M[:, hs], pb.rearrange("p (k m) -> p k m", m=128), t2)]
                    psum.give(n, tm)
                    yield

                def inv_all(h):
                    tm = [tM[h]]
                    for it in range(6):
                        yield from inv_step(it, h, tm)

                tzv = []

                def n_pair(p):
                    c = p // 4
                    n0, e0, we = NE.take()
                    q = BQ[:, c, 2 * (p % 4):2 * (p % 4) + 2, :].rearrange("p a b -> p (a b)")
                    bs = []
                    for h in range(2):
                        n, pb, wt = psum.take()
                        t = mm(pb, q, KT[:, c, 512 * h:512 * h + 512], True, True, tb[0, c], tqk[1, c], wt)
                        bs.append((n, pb, t))
                    yield
                    tm = [red(NMXH[:, 2 * p + h:2 * p + h + 1], bs[h][1], ALU.max, bs[h][2], prev) for h in range(2)]
                    t = tt(dve, NMX[:, p:p + 1], NMXH[:, 2 * p:2 * p + 1], NMXH[:, 2 * p + 1:2 * p + 2], ALU.max, tm)
                    tn = ts(dve, NMX[:, p:p + 1], NMX[:, p:p + 1], -1.0, None, ALU.mult, None, t)
                    te = []
                    for h in range(2):
                        t = act_f(e0[:, 512 * h:512 * h + 512], bs[h][1], ACT.Exp, tn, we,
                                  bias=NMX[:, p:p + 1], acc=NSH[:, 2 * p + h:2 * p + h + 1])
                        psum.give(bs[h][0], t)
                        te.append(t)
                    t = tt(dve, NSUM[:, p:p + 1], NSH[:, 2 * p:2 * p + 1], NSH[:, 2 * p + 1:2 * p + 2], ALU.add, te)
                    ts_ = rcp(NSUM[:, p:p + 1], NSUM[:, p:p + 1], t)
                    yield
                    n1, nt, wn = NTR.take()
                    tt_ = []
                    for h in range(2):
                        n, pb, wt = psum.take()
                        for k in range(4):
                            t = tr(pb[:, 128 * k:128 * k + 128], e0[:, 512 * h + 128 * k:512 * h + 128 * k + 128],
                                   te, wt)
                        t = cp(act if h else dve, nt[:, 4 * h:4 * h + 4, :], pb.rearrange("p (k m) -> p k m", m=128),
                               t, wn, zfree)
                        psum.give(n, t)
                        tt_.append(t)
                    NE.give(n0, t, tt_, ts_)
                    yield
                    n, pb, wt = psum.take()
                    for k in range(8):
                        t = mm(pb[:, 0:32], nt[:, k, :], V[:, k, 32 * p:32 * p + 32], k == 0, k == 7, tt_, tv, wt)
                    NTR.give(n1, t)
                    ta = [ts(dve, ZV[0:64, p, :], pb[0:64, 0:16], NSUM[0:64, p:p + 1], None, ALU.mult, None, t, ts_, prev),
                          ts(dve, ZV[64:128, p, :], pb[64:128, 16:32], NSUM[64:128, p:p + 1], None, ALU.mult, None,
                             t, ts_, prev)]
                    psum.give(n, ta)
                    tzv.extend(ta)
                    yield

                def n_all(r):
                    for p in range(4 * r, 4 * r + 4):
                        yield from n_pair(p)

                zfree = tz
                if b == 0:
                    NMXH, NSH = sm(16), sm(16)
                gens = [inv_all(0), inv_all(1), n_all(0), n_all(1)]
                while gens:
                    for g_ in list(gens):
                        try:
                            next(g_)
                        except StopIteration:
                            gens.remove(g_)
                tcur = list(tzv)
                for it in range(5, -1, -1):
                    n, pb, wt = psum.take()
                    for p in range(8):
                        t = mm(pb[:, 16 * p:16 * p + 16], F[:, it, p, :], ZV[:, p, :], True, True,
                               tF[it, p // 4], tcur, wt)
                    t = cp(dve, ZV, pb[:, 0:128].rearrange("p (a b) -> p a b", b=16), t)
                    psum.give(n, t)
                    tcur = [t]
                n, pb, wt = psum.take()
                for p in range(8):
                    t = mm(pb[:, 16 * p:16 * p + 16], KD[:, p, :], ZV[:, p, :], True, True, tcur, tkd, wt)
                t = tt(dve, ZV, pb[:, 0:128].rearrange("p (a b) -> p a b", b=16),
                       DEN.unsqueeze(2).broadcast_to([128, 8, 16]), ALU.mult, t)
                psum.give(n, t)
                tzb = [tt(dve, ZB[:, :, 16 * x:16 * x + 16], ZV,
                          ZM[:, 16 * x:16 * x + 16].unsqueeze(1).broadcast_to([128, 8, 16]), ALU.mult, t, tc, prev)
                       for x in range(2)]
                last = []
                yfree, rfree, mfree = [], [], [[], []]

                def l_tile(i):
                    tl = []
                    ny, py, wy = None, None, None
                    tys = []
                    for c in range(2):
                        n, pb, wt = psum.take()
                        t = mm(pb, QT[:, c, 128 * i:128 * i + 128], BK[:, c].rearrange("p a b -> p (a b)"),
                               True, True, tqk[0, c], tb[1, c], wt)
                        pv = pb.rearrange("p (a b) -> p a b", b=64)
                        m, le, wl = LE.take()
                        t = red(LMX[:, c, :], pv, ALU.max, t, mfree[c])
                        t = tt(dve, le, pv, LMX[:, c, :].unsqueeze(2).broadcast_to([128, 8, 64]), ALU.subtract, t, wl)
                        psum.give(n, t)
                        mfree[c] = [t]
                        te = act_f(le, le, ACT.Exp, t)
                        ts_ = red(LSM[:, c, :], le, ALU.add, te, rfree)
                        tl.append(ts_)
                        yield
                        n, pb, wt = psum.take()
                        lf = le.rearrange("p a b -> p (a b)")
                        for k in range(4):
                            t = tr(pb[:, 128 * k:128 * k + 128], lf[:, 128 * k:128 * k + 128], te, wt)
                        LE.give(m, t, ts_)
                        m2, lt, wl2 = LT.take()
                        t = cp(act, lt, pb.rearrange("p (k m) -> p k m", m=128), t, wl2)
                        psum.give(n, t)
                        yield
                        ny, py, wy = psum.take()
                        for k in range(4):
                            t2 = mm(py[:, 32 * k:32 * k + 32], lt[:, k, :], ZB[:, 4 * c + k, :], True, True,
                                    t, tzb, wy)
                        LT.give(m2, t2)
                        t = rcp(RIN[:, 8 * c:8 * c + 8], LSM[:, c, :], ts_, rfree)
                        t = tt(dve, YN[:, 128 * c:128 * c + 128].rearrange("p (a b) -> p a b", b=16),
                               py[:, 0:128].rearrange("p (a b) -> p a b", b=16),
                               RIN[:, 8 * c:8 * c + 8].unsqueeze(2).broadcast_to([128, 8, 16]), ALU.mult,
                               t, t2, yfree)
                        psum.give(ny, t)
                        tys.append(t)
                    rfree[:] = tys
                    n, pb, wt = psum.take()
                    for c in range(2):
                        t = tr(pb[:, 128 * c:128 * c + 128], YN[:, 128 * c:128 * c + 128], tys, wt)
                    yfree[:] = [t]
                    t = cp(act, YT, pb[:, 0:256], t, last)
                    psum.give(n, t)
                    n, pb, wt = psum.take()
                    for c in range(2):
                        t2 = mm(pb[:, 0:256], YT[:, 128 * c:128 * c + 128], WP[:, c, :], c == 0, c == 1, t, twp, wt)
                    last[:] = [t2]
                    gi = 8 * b + i
                    t = tt(dve, X[:, gi, :], X[:, gi, :], pb[:, 0:256], ALU.add, t2, tX[gi])
                    psum.give(n, t)
                    tX[gi] = [t]
                    yield

                for i in range(8):
                    for _ in l_tile(i):
                        pass
                prev = [pe.last, dve.last, act.last]

        def ffn1():
            bar = barrier()
            sm_at[0] = sm_keep
            psum = Ring([bank(i) for i in range(8)])
            W1 = [w(4096 * s, 2, FF) for s in range(4)]
            W2 = [w(4096 * s + 2048, 8, D) for s in range(4)]
            wfree = [[], [], [], []]

            def wload(e_):
                s = e_ % 4
                return [load(W1[s], cpf(A["L1_ffn_w1"][e_]), wfree[s]),
                        load(W2[s], cpf(A["L1_ffn_w2"][e_]), wfree[s])]

            twe = [wload(e_) for e_ in range(4)]
            o = 16384
            HHR = Ring([w(o + 2048 * k, 8, 256) for k in range(2)])
            XTR = Ring([w(o + 4096 + 512 * k, 2, 256) for k in range(2)])
            GRR = Ring([w(o + 5120 + 256 * k, 256) for k in range(6)])
            B1 = w(o + 6656, 16, 8)
            B2 = w(o + 6784, 2, 256)
            IOT = w(o + 7296, 1024)
            GQ = w(o + 8320, 256)
            GQT = w(o + 8576, 2, 16)
            BOFF = w(o + 8608, 4, 8)
            IDXF = w(o + 8640, 128)
            GTE = w(o + 8768, 128)
            IDU = w(o + 8896, 64).bitcast(U32)
            MBM = w(o + 8960, 4, 16)
            TT = w(o, 4, 8, 16)
            EE = w(o + 512, 4, 8, 16)
            A2 = w(o + 1024, 8, 4, 16)
            DG = w(o + 1536, 64)
            AT = [w(o + 2048, 1024), w(o + 3072, 1024)]
            IDL = sm(4, 8)
            IDG = sm(4, 8)
            GG = sm(4, 8)
            E32, M32, M1 = sm(4, 8), sm(4, 8), sm(4, 16)
            ET, CM = sm(1), sm(1)
            tgq = load(GQ[0:16], A["L1_ffn_gate_query"])
            tlt = load(ET, A["L1_ffn_log_temp"].partition_broadcast(128))
            tb1 = load(GTE, A["L1_ffn_b1"].rearrange("e (j p) -> (e j) p", p=128))
            t_io = iota(IOT, [[1, 1024]], 0, 0)
            t_bo = iota(BOFF, [[1024, 4], [0, 8]], 0, 0)
            tz, th = layernorm(False, None, psum, bar)
            xnv = XN.rearrange("(i p) d -> p i d", p=128)
            txn = [load(xnv[:, 8 * g:8 * g + 8, :], Z[:, 8 * g:8 * g + 8, :], tz[8 * g:8 * g + 8]) for g in range(4)]
            t = act_f(ET, ET, ACT.Exp, tlt)
            tet = rcp(ET, ET, t)
            n, pb, wt = psum.take()
            for c in range(2):
                t = tr(pb[:, 16 * c:16 * c + 16], GQ[0:16, 128 * c:128 * c + 128], tgq, wt, t_id)
            nb1, pb1, wt1 = psum.take()
            tb1 = tr(pb1[:, 0:128], GTE, tb1, wt1)
            tb1 = cp(dve, B1.rearrange("p e j -> p (e j)"), pb1[:, 0:128], tb1)
            psum.give(nb1, tb1)
            tgt = cp(dve, GQT, pb[:, 0:32].rearrange("p (a b) -> p a b", b=16), t)
            psum.give(n, tgt)
            n, pb, wt = psum.take()
            for i in range(NT):
                for c in range(2):
                    t = mm(pb[:, 16 * i:16 * i + 16], HT[:, c, 128 * i:128 * i + 128], GQT[:, c, :],
                           c == 0, c == 1, th[i // 4], tgt, wt)
            t = ts(dve, TT, pb.rearrange("p (b i e) -> p b i e", b=4, i=8), ET, None, ALU.mult, None, t, tet)
            psum.give(n, t)
            T3 = TT.rearrange("p b i e -> p (b i) e")
            E3 = EE.rearrange("p b i e -> p (b i) e")
            M3 = M32.rearrange("p b i -> p (b i)")
            Q3 = E32.rearrange("p b i -> p (b i)")
            bc3 = lambda v: v.unsqueeze(2).broadcast_to([128, 32, 16])
            tbe = TT.rearrange("p b i e -> p b e i")
            ebe = EE.rearrange("p b i e -> p b e i")
            M1f = M1.rearrange("p b e -> p (b e)")
            MBf = MBM.rearrange("p b e -> p (b e)")
            bc4 = lambda v: v.unsqueeze(2).broadcast_to([128, 4, 8, 16])
            for it in range(6):
                t = red(M3, T3, ALU.max, t)
                t = tt(dve, T3, T3, bc3(M3), ALU.subtract, t)
                t = act_f(EE, TT, ACT.Exp, t)
                t = red(Q3, E3, ALU.add, t)
                t = act_f(Q3, Q3, ACT.Ln, t)
                t = tt(dve, T3, T3, bc3(Q3), ALU.subtract, t)
                t = red(M1, tbe, ALU.max, t)
                n, pb, wt = psum.take()
                t = tr(pb[0:64, 0:128], M1f, t, wt)
                t = red(CM[0:64], pb[0:64, 0:128], ALU.max, t)
                psum.give(n, t)
                t = ts(dve, DG[0:64], IDENT[0:64, 0:64], CM[0:64], None, ALU.mult, None, t)
                n, pb, wt = psum.take()
                t = mm(pb[:, 0:64], ONES[0:64, :], DG[0:64], True, True, t, wt)
                t = cp(dve, MBf, pb[:, 0:64], t)
                psum.give(n, t)
                t = tt(dve, TT, TT, bc4(MBM), ALU.subtract, t)
                t = act_f(EE, TT, ACT.Exp, t)
                t = red(M1, ebe, ALU.add, t)
                n, pb, wt = psum.take()
                t = mm(pb[:, 0:64], ONES[:, :], M1f, True, True, t, wt)
                t = act_f(MBf, pb[:, 0:64], ACT.Ln, t)
                psum.give(n, t)
                t = tt(dve, TT, TT, bc4(MBM), ALU.subtract, t)
            t = act_f(A2.rearrange("p i b e -> p b i e"), TT, ACT.Exp, t)
            tat = []
            for h in range(2):
                n, pb, wt = psum.take()
                for k in range(4):
                    t2 = tr(pb[0:64, 128 * k:128 * k + 128], A2[:, 4 * h + k].rearrange("p b e -> p (b e)"), t, wt)
                t2 = cp(act, AT[0][0:64, 512 * h:512 * h + 512], pb[0:64, :], t2)
                psum.give(n, t2)
                tat.append(t2)
            t = tat
            for r in range(8):
                src, dst = AT[r % 2], AT[1 - r % 2]
                g8 = GTE[0:64, 8 * r:8 * r + 8]
                t = dve(lambda e, g8=g8, src=src: e.max(g8, src[0:64]), t)
                t1 = dve(lambda e, g8=g8, src=src, r=r: e.max_index(IDU[0:64, 8 * r:8 * r + 8], g8, src[0:64]), t)
                if r < 7:
                    t = dve(lambda e, g8=g8, src=src, dst=dst: e.match_replace(dst[0:64], g8, src[0:64], -1.0), t, t1)
            ta = [cp(dve, IDXF[0:64, 64 * x:64 * x + 64], IDU[0:64, :], t1) for x in range(2)]
            tb = cp(dve, GTE[0:64, 64:128], GTE[0:64, 0:64], t)
            n, pb, wt = psum.take()
            t1 = tr(pb[:, 0:64], IDXF[0:64, :], ta, wt)
            t2 = tr(pb[:, 64:128], GTE[0:64, :], tb)
            pi = pb[:, 0:64].rearrange("p (b k x) -> p b k x", b=4, x=2)
            pg = pb[:, 64:128].rearrange("p (b k x) -> p b k x", b=4, x=2)
            ti, tg = [], []
            for x in range(2):
                hs = slice(64 * x, 64 * x + 64)
                ti.append(cp(dve, IDL[hs], pi[hs, :, :, x], t1, t2))
                tg.append(ts(dve, GG[hs], pg[hs, :, :, x], 0.5, None, ALU.mult, None, t2))
            psum.give(n, ti, tg)
            tig = tt(dve, IDG.bitcast(U32), IDL, BOFF, ALU.add, ti, t_bo)
            tlist = [tig, tg, ti]
            Y = Z[:, :, :].rearrange("p (k b) d -> p k b d", b=4)
            tY = []
            thead = [dve.last, act.last, pe.last]
            for ep in range(8):
                es = (2 * ep, 2 * ep + 1)
                xts = [XTR.take() for _ in range(2)]
                txt = [[], []]
                for b in range(4):
                    n, gr, wg = GRR.take()
                    tgr = pool.dma(lambda e, b=b, ep=ep, gr=gr: e.indirect_dma_start(
                        out=gr, out_offset=None, in_=XN,
                        in_offset=bass.IndirectOffsetOnAxis(ap=IDG.bitcast(U32)[:, b, ep:ep + 1], axis=0)),
                        tig, wg, txn)
                    nb, pb, wt = psum.take()
                    for c in range(2):
                        t = tr(pb[:, 128 * c:128 * c + 128], gr[:, 128 * c:128 * c + 128], tgr, wt)
                    GRR.give(n, t)
                    tc_ = []
                    for x in range(2):
                        t2 = cp(act, xts[x][1][:, :, 64 * b:64 * b + 64],
                                pb[:, 0:256].rearrange("p (c y s) -> p c y s", c=2, y=2)[:, :, x, :],
                                t, xts[x][2], thead)
                        txt[x].append(t2)
                        tc_.append(t2)
                    psum.give(nb, tc_)
                hhs = []
                for x in range(2):
                    e_ = es[x]
                    s = e_ % 4
                    m, hh, wh = HHR.take()
                    hhs.append((m, hh))
                    thh = []
                    for j2 in range(4):
                        n, pb, wt = psum.take()
                        for jj in range(2):
                            j = 2 * j2 + jj
                            for c in range(2):
                                t = mm(pb[:, 256 * jj:256 * jj + 256], W1[s][:, c, 128 * j:128 * j + 128],
                                       xts[x][1][:, c, :], c == 0, c == 1, txt[x], twe[e_], wt)
                        for jj in range(2):
                            j = 2 * j2 + jj
                            t2 = act_f(hh[:, j, :], pb[:, 256 * jj:256 * jj + 256], ACT.Gelu_apprx_tanh, t, wh,
                                       thead, tb1, bias=B1[:, e_, j:j + 1])
                            thh.append(t2)
                        psum.give(n, t2)
                    XTR.give(xts[x][0], t)
                    hhs[x] += (thh,)
                tb2 = [load(B2[0:1, x], A["L1_ffn_b2"][es[x]:es[x] + 1, :], tY[-1:] and tY[-1]) for x in range(2)]
                ty = []
                for b in range(4):
                    n, pb, wt = psum.take()
                    for j in range(8):
                        for x in range(2):
                            t = mm(pb[64 * x:64 * x + 64, 0:D], hhs[x][1][:, j, 64 * b:64 * b + 64],
                                   W2[es[x] % 4][:, j, :], j == 0, False, hhs[x][2], twe[es[x]], wt)
                    for x in range(2):
                        t = mm(pb[64 * x:64 * x + 64, 0:D], ONES[0:1, 0:64], B2[0:1, x], False, True, tb2[x])
                    t2 = ts(dve, Y[:, ep, b, :], pb[:, 0:D], GG[:, b, ep:ep + 1], None, ALU.mult, None, t, tg, txn)
                    psum.give(n, t2)
                    ty.append(t2)
                tY.append(ty)
                for x in range(2):
                    HHR.give(hhs[x][0], t)
                    wfree[es[x] % 4] = [t]
                    if es[x] + 4 < 16:
                        twe.append(wload(es[x] + 4))
            thead = [pe.last]
            SR = Ring([HT[:, :, :].rearrange("p c t -> p (c t)")[:, 1024 * k:1024 * k + 1024] for k in range(8)])
            for b in range(4):
                ss = []
                for ep in range(8):
                    n, s_, wt = SR.take()
                    t = ts(dve, s_, IOT, IDL[:, b, ep:ep + 1], None, ALU.is_equal, None, wt, t_io, thead, ti)
                    ss.append((n, s_, t))
                for i in range(8):
                    n, pb, wt = psum.take()
                    for ep in range(8):
                        t = mm(pb[:, 0:D], ss[ep][1][:, 128 * i:128 * i + 128], Y[:, ep, b, :], ep == 0, ep == 7,
                               ss[ep][2], tY[ep], wt)
                    gi = 8 * b + i
                    t2 = tt(dve, X[:, gi, :], X[:, gi, :], pb[:, 0:D], ALU.add, t, tX[gi])
                    psum.give(n, t2)
                    tX[gi] = [t2]
                for n, _, _ in ss:
                    SR.give(n, t)


        def attn1():
            bar = barrier()
            sm_at[0] = sm_keep
            psum = Ring([bank(i) for i in range(8)])
            QM = {(0, 0): (0, 1), (1, 0): (1, -1), (2, 0): (2, -1), (3, 0): (3, -1),
                  (1, 1): (0, 1), (0, 1): (1, 1), (3, 1): (2, 1), (2, 1): (3, -1),
                  (2, 2): (0, 1), (3, 2): (1, -1), (0, 2): (2, 1), (1, 2): (3, 1),
                  (3, 3): (0, 1), (2, 3): (1, 1), (1, 3): (2, -1), (0, 3): (3, 1)}
            BS = [(1, -1, -1, -1), (1, 1, 1, -1), (1, -1, 1, 1), (1, 1, -1, 1)]
            QS = Ring([w(2048 * k, 2048).bitcast(BF16).rearrange("p (h t) -> p h t", h=4) for k in range(2)])
            KS = Ring([w(4096 + 2048 * k, 2048).bitcast(BF16).rearrange("p (h t) -> p h t", h=4) for k in range(2)])
            o = 8192
            V = w(o, 8 * 272 + 16)
            PR = Ring([w(o + 2192 + 4096 * k, 4, 1024) for k in range(2)])
            o += 2192 + 8192
            QL = w(o, 2, 1024)
            N2 = w(o + 2048, 1024)
            SQ = w(o + 3072, 2, 1024)
            o += 5120
            OC = w(o, 1024)
            ON = w(o + 1024, 1024)
            o += 2048
            SQM, SDM = w(o, 128), w(o + 128, 128)
            SGN = w(o + 256, 2, 4)
            BQK = w(o + 264, 2, 2, 4)
            BB = w(o + 280, 4)
            BVO = w(o + 284, 2, 256)
            JB, JK = OC[:, 0:256], OC[:, 256:512]
            BT = OC[:, 512:768].rearrange("p (k o) -> p k o", k=4)
            WQ = w(o + 796, 2, 256)
            assert o + 1308 <= 27300
            CB = sm(1)
            tz, th = layernorm(False, None, psum, bar)
            zdone = [pe.last]
            zf = Z[:, :, :].rearrange("p a b -> p (a b)")
            WKK = zf[:, 0:512].rearrange("p (c n) -> p c n", c=2)
            WV = zf[:, 512:1024].rearrange("p (c n) -> p c n", c=2)
            WO = zf[:, 1024:2048].rearrange("p (g n) -> p g n", g=4)
            PT = {}
            for x in range(2):
                for k in range(3):
                    off = 2048 + 1024 * (3 * x + k)
                    v = zf[:, off:off + 1024].bitcast(BF16).rearrange("p (c t) -> p c t", c=2)
                    PT[x, k] = v
            tw = {}
            for nm, dst in (("q", WQ), ("k", WKK), ("v", WV)):
                src = A[f"L1_attn_{nm}W"]
                tl = []
                for (ci, co), (wi, sg) in QM.items():
                    d = dst[64 * (ci % 2):64 * (ci % 2) + 64, ci // 2, 64 * co:64 * co + 64]
                    t = load(d, src[wi], zdone)
                    if sg < 0:
                        t = ts(pool, d, d, -1.0, None, ALU.mult, None, t)
                    tl.append(t)
                tw[nm] = tl
            t0 = mset(pool, WO, 0.0, zdone)
            tl = []
            for (ci, co), (wi, sg) in QM.items():
                tj = [load(WO[32 * j:32 * j + 16, ci, 64 * co:64 * co + 64], A["L1_attn_oW"][wi][16 * j:16 * j + 16, :],
                           t0) for j in range(4)]
                if sg < 0:
                    d = WO[:, ci, 64 * co:64 * co + 64]
                    tj = [ts(pool, d, d, -1.0, None, ALU.mult, None, tj)]
                tl += tj
            tw["o"] = tl
            t = mset(pool, SQM, 0.0)
            for base in (0, 64, -64):
                t = asel(SQM, [[-1, 128]], ALU.not_equal, 1.0, base, 1, t)
            tc = [t]
            t = mset(pool, SDM, 0.0)
            tc.append(asel(SDM.rearrange("p (j i) -> p j i", j=4), [[-32, 4], [0, 32]], ALU.not_equal, 1.0, -16, 1, t))
            tsg = []
            for c in range(2):
                for x in range(2):
                    for k in range(4):
                        tsg.append(mset(pool, SGN[64 * x:64 * x + 64, c, k:k + 1], float(BS[2 * c + x][k])))
            BI = {}
            for x, nm in enumerate(("q", "k")):
                tl = [load(BB[64 * y:64 * y + 64], A[f"L1_attn_{nm}b"].rearrange("k o -> o k"),
                           BI.get("t")) for y in range(2)]
                t = tt(dve, BQK[:, x], SGN, BB.unsqueeze(1).broadcast_to([128, 2, 4]), ALU.mult, tl, tsg)
                BI["t"] = t
                dst = sm(2)
                BI[x] = (dst, red(dst, BQK[:, x], ALU.add, t))
            tbt = None
            for x, nm in enumerate(("v", "o")):
                t = load(BT, A[f"L1_attn_{nm}b"].rearrange("k o -> (k o)").partition_broadcast(128).rearrange(
                    "p (k o) -> p k o", k=4), tbt)
                tl = []
                for co in range(4):
                    d = BVO[:, x, 64 * co:64 * co + 64]
                    u = t
                    u = cp(pool, d, BT[:, 0, :], u)
                    for k in range(1, 4):
                        u = tt(pool, d, d, BT[:, k, :], ALU.add if BS[co][k] > 0 else ALU.subtract, u)
                    tl.append(u)
                tbt = tl
                BI[nm] = tl
            t = load(JB, A["L1_attn_J"].partition_broadcast(128))
            t = ts(dve, JK, JB, float(1 / (2 * np.pi)), None, ALU.mult, None, t)
            t = ts(dve, JK, JK, 12582912.0, None, ALU.add, None, t)
            t = ts(dve, JK, JK, -12582912.0, None, ALU.add, None, t)
            t = stt(JB, JK, -6.28125, JB, ALU.mult, ALU.add, t)
            t = stt(JB, JK, -float(2 * np.pi - 6.28125), JB, ALU.mult, ALU.add, t)
            t = ts(dve, JB, JB, 3.1415925, -3.1415925, ALU.min, ALU.max, t)
            t = act_f(JK, JB, ACT.Sin, t, acc=CB)
            tcb = ts(dve, CB, CB, 0.1 / 256.0, None, ALU.mult, None, t)
            tob = []
            for i in range(NT):
                t = tt(pool, X[:, i, :], X[:, i, :], BVO[:, 1, :], ALU.add, BI["o"], tz[i], tX[i])
                tX[i] = [t]
            tvp = mset(pool, V, 1.0)
            qfree, ptfree = [], {(0, k): [] for k in range(3)} | {(1, k): [] for k in range(3)}
            vfree = [tvp]
            sfree = []
            tpt = {}
            v4 = V[:, 0:2176].rearrange("p (t h e) -> p t h e", t=8, e=17)
            pending = []

            def prep_qk(b):
                H0 = 1024 * b
                for x, W in ((0, WQ), (1, WKK)):
                    tl = []
                    for h in range(2):
                        for c in range(2):
                            n, pb, wt = psum.take()
                            for k in range(2):
                                t = mm(pb, W[:, k, 128 * c:128 * c + 128], HT[:, k, H0 + 512 * h:H0 + 512 * h + 512],
                                       k == 0, k == 1, tw["qk"[x]], th[2 * b + h], wt)
                            t = ts(dve, QL[:, c, 512 * h:512 * h + 512], pb, BI[x][0][:, c:c + 1], None, ALU.add,
                                   None, t, BI[x][1], qfree)
                            psum.give(n, t)
                            tl.append(t)
                    tsq = tt(pool, SQ, QL, QL, ALU.mult, tl, sfree)
                    tn = []
                    for h in range(2):
                        n, pb, wt = psum.take()
                        for k in range(2):
                            t = mm(pb, SQM, SQ[:, k, 512 * h:512 * h + 512], k == 0, k == 1, tsq, wt, tc)
                        t = ts(dve, N2[:, 512 * h:512 * h + 512], pb, 1e-6, None, ALU.add, None, t, qfree)
                        psum.give(n, t)
                        tn.append(t)
                    t = act_f(N2, N2, ACT.Sqrt, tn)
                    t = rcp(N2, N2, t)
                    t = tt(dve, QL, QL, N2.unsqueeze(1).broadcast_to([128, 2, 1024]), ALU.mult, t)
                    t1 = cp(dve, PT[x, 0], QL, t, ptfree[x, 0], zdone)
                    t2 = tt(dve, QL, QL, PT[x, 0], ALU.subtract, t1)
                    t3 = cp(dve, PT[x, 1], QL, t2, ptfree[x, 1], zdone)
                    t4 = tt(dve, PT[x, 2], QL, PT[x, 1], ALU.subtract, t3, ptfree[x, 2], zdone)
                    tpt[x] = [t1, t3, t4]
                    qfree[:] = [t4]
                    sfree[:] = [pe.last]
                    for k in range(3):
                        ptfree[x, k] = []

            PARTS = ((0, 0, 1, 1, 0, 2), (0, 1, 0, 1, 2, 0))

            def stack(b, g):
                res = []
                for x, RG in ((0, QS), (1, KS)):
                    n, buf, wt = RG.take()
                    tl = []
                    for bl in range(6):
                        k = PARTS[x][bl]
                        for j in range(4):
                            p0 = 64 * (g % 2) + 16 * j
                            t = load(buf[16 * bl:16 * bl + 16, j, :], PT[x, k][p0:p0 + 16, g // 2, :],
                                     tpt[x][k], wt)
                            tl.append(t)
                            ptfree[x, k] = ptfree[x, k] + [t]
                    res.append((n, buf, tl))
                return res

            def prep_v(b):
                H0 = 1024 * b
                tl = []
                for i in range(8):
                    n, pb, wt = psum.take()
                    for k in range(2):
                        t = mm(pb[:, 0:256], HT[:, k, H0 + 128 * i:H0 + 128 * i + 128], WV[:, k, :], k == 0, k == 1,
                               tw["v"], th[2 * b + i // 4], wt)
                    t = tt(dve, v4[:, i, :, 0:16], pb[:, 0:256].rearrange("p (h e) -> p h e", e=16),
                           BVO[:, 0, :].rearrange("p (h e) -> p h e", e=16), ALU.add, t, BI["v"], vfree)
                    psum.give(n, t)
                    tl.append(t)
                return tl

            for b in range(4):
                psum = Ring([bank(i) for i in range(8)])
                for ln in (pe,):
                    ln.pending += [t for t in (act.last, dve.last) if t]
                for t in (act.last, dve.last):
                    t.used = True
                prep_qk(b)
                tv = prep_v(b)
                for t in (act.last, dve.last):
                    t.used = True
                pe.pending += [act.last, dve.last]
                SP_ = Ring([pair(0), pair(2), pair(4)])
                OP = pair(6)
                nxt = stack(b, 0)
                ofree = []
                for g in range(4):
                    (nq, qs, tq), (nk, ks, tk_) = nxt
                    if g < 3:
                        nxt = stack(b, g + 1)
                    tpv = None

                    def pv(kt, m, pr, te):
                        for h in range(2):
                            for j in range(4):
                                hd = 4 * g + j
                                base = 272 * kt + 17 * hd
                                t = mm(OP[32 * j:32 * j + 32, 512 * h:512 * h + 512], V[:, base:base + 32],
                                       pr[:, j, 512 * h:512 * h + 512], kt == 0, kt == 7, te, tv, ofree)
                        PR.give(m, t)
                        return t

                    prevp = None
                    for kt in range(8):
                        m, pr, wp = PR.take()
                        te = []
                        for j in range(4):
                            n, sp_, wt = SP_.take()
                            for h in range(2):
                                t = mm(sp_[:, 512 * h:512 * h + 512], ks[0:96, j, 128 * kt:128 * kt + 128],
                                       qs[0:96, j, 512 * h:512 * h + 512], True, True, tq, tk_, wt)
                            t = act_f(pr[:, j, :], sp_, ACT.Exp, t, wp, tcb, bias=CB, scale=0.25)
                            SP_.give(n, t)
                            te.append(t)
                        if prevp is not None:
                            pv(*prevp)
                        prevp = (kt, m, pr, te)
                    tl = pe.last
                    QS.give(nq, tl)
                    KS.give(nk, tl)
                    t = pv(*prevp)
                    toc = cp(dve, OC, OP, t, ofree)
                    ofree = [toc]
                    n, sp_, wt = SP_.take()
                    for h in range(2):
                        t = mm(sp_[:, 512 * h:512 * h + 512], SDM, OC[:, 512 * h:512 * h + 512], True, True, toc, wt, tc)
                    t = rcp(ON, sp_, t, pending)
                    SP_.give(n, t)
                    ton = tt(dve, ON, ON, OC, ALU.mult, t)
                    for i2 in range(2):
                        n, sp_, wt = SP_.take()
                        for i in range(4):
                            t = mm(sp_[:, 256 * i:256 * i + 256], ON[:, 512 * i2 + 128 * i:512 * i2 + 128 * i + 128],
                                   WO[:, g, :], True, True, ton, tw["o"], wt)
                        tx = []
                        gi = 8 * b + 4 * i2
                        t2 = tt(dve, X[:, gi:gi + 4, :], X[:, gi:gi + 4, :],
                                sp_.rearrange("p (i d) -> p i d", i=4), ALU.add, t, tX[gi:gi + 4])
                        for i in range(4):
                            tX[gi + i] = [t2]
                        SP_.give(n, t2)
                    pending = [t]
                    ofree = ofree + [ton]
                vfree = [pe.last]
                qfree[:] = qfree + [pe.last]

        phases = [lambda: ffn0(True), attn0, lambda: ffn0(span[0] == 2), ffn1, attn1, ffn1]
        for ph in phases[span[0]:span[1]]:
            ph()
        ov = out.rearrange("b (i p) d -> p (b i) d", p=128)
        for g in range(4):
            sp.dma(lambda e, g=g: e.dma_start(ov[:, 8 * g:8 * g + 8, :], X[:, 8 * g:8 * g + 8, :]),
                   tX[8 * g:8 * g + 8])
        ends = [t for ln in lanes for t in ln.dlast if t]
        for ln in lanes:
            ln.count()
        block = ctx.enter_context(nc.Block())

        @block.sync
        def _(e):
            sp.replay(e)
            for t in ends:
                e.wait_ge(t.sem, t.val)

        @block.tensor
        def _(e):
            pe.replay(e)

        @block.scalar
        def _(e):
            act.replay(e)

        @block.vector
        def _(e):
            dve.replay(e)

        @block.gpsimd
        def _(e):
            pool.replay(e)


INPUTS = ['L0_attn_x', 'L0_attn_W_attn', 'L0_attn_W_proj', 'L0_ffn_ln_g', 'L0_ffn_ln_b', 'L0_ffn_Wr', 'L0_ffn_W1',
          'L0_ffn_W3', 'L0_ffn_W2', 'L0_ffn_W1s', 'L0_ffn_W3s', 'L0_ffn_W2s', 'L1_attn_qW', 'L1_attn_qb',
          'L1_attn_kW', 'L1_attn_kb', 'L1_attn_vW', 'L1_attn_vb', 'L1_attn_oW', 'L1_attn_ob', 'L1_attn_J',
          'L1_ffn_gate_query', 'L1_ffn_log_temp', 'L1_ffn_w1', 'L1_ffn_b1', 'L1_ffn_w2', 'L1_ffn_b2']


def build(nc, arrays, span=(0, 6)):
    A = {}
    for name, a in arrays.items():
        A[name] = nc.dram_tensor(name + "_dram", a.shape, mybir.dt.from_np(a.dtype), kind="ExternalInput").ap()
    out = nc.dram_tensor("out_dram", (4, 1024, 256), F32, kind="ExternalOutput").ap()
    macaron_kernel(nc, A, out, span)


def kernel(**inputs):
    import concourse.bacc as bacc
    from concourse.bass_utils import run_bass_kernel_spmd

    nc = bacc.Bacc("TRN2", target_bir_lowering=False, num_devices=1)
    arrays = {n: np.ascontiguousarray(inputs[n]) for n in INPUTS}
    arrays["L1_ffn_log_temp"] = arrays["L1_ffn_log_temp"].reshape(1)
    build(nc, arrays)
    r = run_bass_kernel_spmd(nc, [{n + "_dram": a for n, a in arrays.items()}], core_ids=[0])
    return r.results[0]["out_dram"]
```
